# Optimizing a Trainium2 kernel written in Bass

```python
import numpy as np
import jax
import jax.numpy as jnp

def _softmax(x, axis=-1):
    return jax.nn.softmax(x, axis=axis)

def _gelu(x):
    return jax.nn.gelu(x, approximate=True)

def _silu(x):
    return jax.nn.silu(x)

def _sigmoid(x):
    return jax.nn.sigmoid(x)

def _layernorm(x, axis=-1, eps=1e-05):
    m = jnp.mean(x, axis=axis, keepdims=True)
    v = jnp.var(x, axis=axis, keepdims=True)
    return (x - m) / jnp.sqrt(v + eps)

def _scatter_add(tgt, idx, src, axis=0):
    return tgt.at[idx].add(src)

def _segment_sum(src, seg, n):
    return jax.ops.segment_sum(src, seg, n)
kernel_name = 'mk_adj_resnorm_d1_adj_r2_c05e53'

def setup_inputs(seed: int=0):
    np.random.seed(seed)
    _w = jnp.asarray

    def _rec_inputs():
        import jax
        import jax.numpy as jnp
        _gk = jax.random.key(seed)
        x = -0.0004039 + 1 * jax.random.normal(jax.random.fold_in(_gk, 1), (32, 256, 384), jnp.float32)
        _a = jax.random.bernoulli(jax.random.fold_in(_gk, 2), 0.03125, (32, 256, 256))
        _af = _a.astype(jnp.float32)
        adj = _af
        return (x, adj)
    x, adj = _rec_inputs()

    def _L0_gnn_setup():
        import jax, jax.numpy as jnp
        import numpy as np
        B, L, H = (8, 1024, 384)
        LN_EPS = 1e-12
        key = jax.random.key(seed)
        ks = jax.random.split(key, 10)
        hidden_state = jax.random.normal(ks[0], (B, L, H), dtype=jnp.float32)
        adjacency = jax.random.randint(ks[1], (B, L, L), 0, 2).astype(jnp.float32)
        bound = 1.0 / np.sqrt(H)
        W_left = jax.random.normal(ks[2], (H, H), dtype=jnp.float32) * np.sqrt(2.0 / (H + H))
        b_left = jax.random.uniform(ks[3], (H,), minval=-bound, maxval=bound, dtype=jnp.float32)
        W_self = jax.random.normal(ks[4], (H, H), dtype=jnp.float32) * np.sqrt(2.0 / (H + H))
        b_self = jax.random.uniform(ks[5], (H,), minval=-bound, maxval=bound, dtype=jnp.float32)
        W_right = jax.random.normal(ks[6], (H, H), dtype=jnp.float32) * np.sqrt(2.0 / (H + H))
        b_right = jax.random.uniform(ks[7], (H,), minval=-bound, maxval=bound, dtype=jnp.float32)
        gamma = jnp.ones((H,), dtype=jnp.float32)
        beta = jnp.zeros((H,), dtype=jnp.float32)
        return {'hidden_state': hidden_state, 'adjacency': adjacency, 'W_left': W_left, 'b_left': b_left, 'W_self': W_self, 'b_self': b_self, 'W_right': W_right, 'b_right': b_right, 'gamma': gamma, 'beta': beta}
    _L0_gnn_all = _L0_gnn_setup()
    _L0_gnn_in = {k: v for k, v in _L0_gnn_all.items() if k in ('W_left', 'b_left', 'W_self', 'b_self', 'W_right', 'b_right', 'gamma', 'beta')}
    del _L0_gnn_all
    return {'x': x, 'adj': adj, 'L0_gnn_W_left': _L0_gnn_in['W_left'], 'L0_gnn_b_left': _L0_gnn_in['b_left'], 'L0_gnn_W_self': _L0_gnn_in['W_self'], 'L0_gnn_b_self': _L0_gnn_in['b_self'], 'L0_gnn_W_right': _L0_gnn_in['W_right'], 'L0_gnn_b_right': _L0_gnn_in['b_right'], 'L0_gnn_gamma': _L0_gnn_in['gamma'], 'L0_gnn_beta': _L0_gnn_in['beta']}

def reference(x, adj, L0_gnn_W_left, L0_gnn_b_left, L0_gnn_W_self, L0_gnn_b_self, L0_gnn_W_right, L0_gnn_b_right, L0_gnn_gamma, L0_gnn_beta):
    import jax
    import jax.numpy as jnp

    def _L0_gnn_ref(hidden_state, adjacency, W_left, b_left, W_self, b_self, W_right, b_right, gamma, beta):
        import jax, jax.numpy as jnp
        import numpy as np
        B, L, H = (8, 1024, 384)
        LN_EPS = 1e-12
        h = hidden_state
        d = h.shape[-1]
        n = h.shape[1]
        u = jnp.einsum('bld,bmd->blm', h, h) / jnp.sqrt(jnp.asarray(d, h.dtype))
        p = jax.nn.softmax(u, axis=-1)
        delta = p * adjacency
        attn = delta / (jnp.sum(delta, axis=2, keepdims=True) + 1e-10)
        h_left = jnp.einsum('bld,ed->ble', h, W_left) + b_left
        h_self = jnp.einsum('bld,ed->ble', h, W_self) + b_self
        h_right = jnp.einsum('bld,ed->ble', h, W_right) + b_right
        i = jnp.arange(n)[:, None]
        j = jnp.arange(n)[None, :]
        attn_left = jnp.where(j > i, attn, 0.0)
        attn_right = jnp.where(j < i, attn, 0.0)
        diag_a = jnp.diagonal(attn, axis1=1, axis2=2)
        ctx = jnp.einsum('blm,bmd->bld', attn_left, h_left) + diag_a[..., None] * h_self + jnp.einsum('blm,bmd->bld', attn_right, h_right)
        mu = jnp.mean(ctx, axis=-1, keepdims=True)
        var = jnp.mean(jnp.square(ctx - mu), axis=-1, keepdims=True)
        o = (ctx - mu) / jnp.sqrt(var + LN_EPS) * gamma + beta
        return jax.nn.relu(o)
    x = _layernorm(x + _L0_gnn_ref(x, adj, L0_gnn_W_left, L0_gnn_b_left, L0_gnn_W_self, L0_gnn_b_self, L0_gnn_W_right, L0_gnn_b_right, L0_gnn_gamma, L0_gnn_beta), axis=-1)
    return x

_drawn_inputs = setup_inputs


def setup_inputs(seed=0):
    import zlib

    import numpy as np

    out = dict(_drawn_inputs(seed))
    spreads = {'L0_gnn_gamma': (1.0, 0.2), 'L0_gnn_beta': (0.0, 0.1)}
    factors = {'L0_gnn_b_self': 8.0}
    for name, (base, spread) in spreads.items():
        noise = np.random.default_rng([zlib.crc32(name.encode()), seed]).standard_normal(out[name].shape)
        drawn = base * np.exp(spread * noise) if base else spread * noise
        out[name] = jnp.asarray(drawn.astype(out[name].dtype))
    for name, factor in factors.items():
        out[name] = (out[name] * factor).astype(out[name].dtype)
    return out
```

```python
from contextlib import ExitStack

import concourse.bass as bass
from concourse import mybir

P = 128
UNROLL = 4
F32 = mybir.dt.float32
F32R = mybir.dt.float32r
ALU = mybir.AluOpType
ACT = mybir.ActivationFunctionType
AX = mybir.AxisListType.X
LN1_EPS = 1e-12
LN2_EPS = 1e-5
SUM_EPS = 1e-10


class Batch:

    def __init__(self, turn, u):
        self.turn, self.u = turn, u
        self.fixed = isinstance(turn, int)
        self.b = UNROLL * turn + u if self.fixed else None

    def n(self, per, c=0):
        return self.turn * (UNROLL * per) + (self.u * per + c)

    def uses(self, ring, c=0):
        return self.turn * (16 * UNROLL // ring) + 16 * (self.u // ring + c)


def every_batch(eng, batches, one):
    turns = batches // UNROLL
    for u in range(UNROLL):
        one(Batch(0, u))
    with eng.Fori(1, turns - 1) as turn:
        for u in range(UNROLL):
            one(Batch(turn, u))
    for u in range(UNROLL):
        one(Batch(turns - 1, u))


def gnn_resnorm(nc, x, adj, wt_left, b_left, wt_self, b_self, wt_right, b_right, gamma, beta, out):
    BATCHES, L, H = x.shape
    T = L // P
    C = H // P
    assert T == 2 and C == 3 and BATCHES % UNROLL == 0
    SCALE = 1.0 / float(H) ** 0.5
    LEFT, RIGHT, SELF = range(3)
    GROUPS = [(LEFT, 0), (RIGHT, 0), (LEFT, 1), (RIGHT, 1), (SELF, 0), (SELF, 1)]
    NG, NSPLIT, PBANKS = 6, 4, 3
    LAST = BATCHES - 1
    BLOCKS = [(0, 0), (1, 1), (1, 0), (0, 1)]
    FULL, MASK_LEFT, MASK_RIGHT = range(3)
    ATTEND = [
        [(MASK_LEFT, 0, 0), (MASK_RIGHT, 0, 1), (FULL, 2, 2)],
        [(FULL, 3, 1), (MASK_LEFT, 1, 2), (MASK_RIGHT, 1, 3)],
    ]

    with ExitStack() as ctx:
        def sb(name, shape, dt=F32):
            return ctx.enter_context(nc.sbuf_tensor(name, shape, dt))

        def psum(name, shape):
            return ctx.enter_context(nc.psum_tensor(name, shape, F32))

        def sem(name):
            return ctx.enter_context(nc.semaphore(name))

        ident = sb("ident", [P, P])
        minus_half = sb("minus_half", [P, T])
        w_raw = [sb(f"w_raw{w}", [P, C, H]) for w in range(3)]
        w_hi = [sb(f"w_hi{w}", [P, C, H], F32R) for w in range(3)]
        w_lo = [sb(f"w_lo{w}", [P, C, H], F32R) for w in range(3)]
        bias = [sb(f"bias{w}", [P, H]) for w in range(3)]
        gamma_sb = sb("gamma_sb", [P, H])
        beta_sb = sb("beta_sb", [P, H])
        x_sb = [sb(f"x_sb{i}", [P, T, H]) for i in range(UNROLL)]
        adj_sb = [sb(f"adj_sb{i}", [P, T, L]) for i in range(UNROLL)]
        xt_hi = [sb(f"xt_hi{i}", [P, C, L], F32R) for i in range(2)]
        xt_lo = [sb(f"xt_lo{i}", [P, C, L], F32R) for i in range(2)]
        diag = [sb(f"diag{i}", [P, T]) for i in range(2)]
        recip = [sb(f"recip{i}", [P, T]) for i in range(2)]
        out_sb = [sb(f"out_sb{i}", [P, T, H]) for i in range(2)]
        row_max = sb("row_max", [P, T])
        neg_max = sb("neg_max", [P, T])
        z_sum = sb("z_sum", [P, T])
        e_sb = sb("e_sb", [P, T, L])
        delta = sb("delta", [P, T, L])
        s_sum = sb("s_sum", [P, T])
        denom = sb("denom", [P, T])
        on_diag = sb("on_diag", [P, T, P])
        dt_full = sb("dt_full", [P, 2, T * T, P], F32R)
        dt_left = sb("dt_left", [P, 2, T, P], F32R)
        dt_right = sb("dt_right", [P, 2, T, P], F32R)
        proj = sb("proj", [P, NSPLIT, H])
        proj_hi = sb("proj_hi", [P, NSPLIT, H], F32R)
        proj_lo = sb("proj_lo", [P, NSPLIT, H], F32R)
        proj_self = sb("proj_self", [P, T, H])
        context = sb("context", [P, T, H])
        stats1 = sb("stats1", [P, T, 6])
        mv1 = sb("mv1", [P, T, 2])
        recip_sq = sb("recip_sq", [P, T])
        var1 = sb("var1", [P, T])
        var1_eps = sb("var1_eps", [P, T])
        pow1 = sb("pow1", [P, T])
        scale1 = sb("scale1", [P, T])
        shift1 = sb("shift1", [P, T])
        normed = sb("normed", [P, T, H])
        scaled = sb("scaled", [P, T, H])
        shifted = sb("shifted", [P, T, H])
        y_sb = sb("y_sb", [P, T, H])
        stats2 = sb("stats2", [P, T, 6])
        mv2 = sb("mv2", [P, T, 2])
        var2_eps = sb("var2_eps", [P, T])
        scale2 = sb("scale2", [P, T])
        shift2 = sb("shift2", [P, T])
        ps_turn = psum("ps_turn", [P, C, P])
        ps_scores = psum("ps_scores", [P, T, L])
        ps_dt = psum("ps_dt", [P, T * T, P])
        ps_proj = [psum(f"ps_proj{i}", [P, 512]) for i in range(PBANKS)]
        ps_ctx = [psum(f"ps_ctx{i}", [P, 512]) for i in range(T)]

        x_loaded = [sem(f"x_loaded{i}") for i in range(UNROLL)]
        adj_loaded = [sem(f"adj_loaded{i}") for i in range(UNROLL)]
        w_loaded = [sem(f"w_loaded{w}") for w in range(3)]
        vectors_loaded = sem("vectors_loaded")
        stored = [sem(f"stored{i}") for i in range(2)]
        ident_zeroed = sem("ident_zeroed")
        ident_ready = sem("ident_ready")
        minus_half_ready = sem("minus_half_ready")
        w_hi_ready = sem("w_hi_ready")
        w_lo_ready = sem("w_lo_ready")
        turned = sem("turned")
        scores_ready = sem("scores_ready")
        dt_ready = sem("dt_ready")
        proj_ready = sem("proj_ready")
        ctx_ready = sem("ctx_ready")
        xt_hi_ready = sem("xt_hi_ready")
        exp_ready = sem("exp_ready")
        dt_hi_ready = sem("dt_hi_ready")
        proj_hi_ready = sem("proj_hi_ready")
        normed_ready = sem("normed_ready")
        out_ready = sem("out_ready")
        xt_lo_ready = sem("xt_lo_ready")
        row_max_ready = sem("row_max_ready")
        neg_max_ready = sem("neg_max_ready")
        delta_ready = sem("delta_ready")
        denom_ready = sem("denom_ready")
        softmax_done = sem("softmax_done")
        dt_lo_ready = sem("dt_lo_ready")
        proj_biased = sem("proj_biased")
        context_ready = sem("context_ready")
        stats1_ready = sem("stats1_ready")
        mv1_ready = sem("mv1_ready")
        recip_sq_ready = sem("recip_sq_ready")
        var1_ready = sem("var1_ready")
        var1_eps_ready = sem("var1_eps_ready")
        scale1_ready = sem("scale1_ready")
        shift1_ready = sem("shift1_ready")
        y_ready = sem("y_ready")
        stats2_ready = sem("stats2_ready")
        mv2_ready = sem("mv2_ready")
        var2_eps_ready = sem("var2_eps_ready")
        shift2_ready = sem("shift2_ready")
        proj_lo_ready = sem("proj_lo_ready")
        triangles_ready = sem("triangles_ready")
        pow1_ready = sem("pow1_ready")
        scaled_ready = sem("scaled_ready")
        shifted_ready = sem("shifted_ready")
        scale2_ready = sem("scale2_ready")

        x_rows = x.rearrange("b (t p) h -> b p t h", p=P)
        adj_rows = adj.rearrange("b (t p) m -> b p t m", p=P)
        out_rows = out.rearrange("b (t p) h -> b p t h", p=P)

        block = ctx.enter_context(nc.Block())

        @block.sync
        def _(sp):
            def load(b, slot):
                sp.dma_start(x_sb[slot][:], x_rows[b]).then_inc(x_loaded[slot], 16)
                sp.dma_start(adj_sb[slot][:], adj_rows[b]).then_inc(adj_loaded[slot], 16)

            sp.dma_start(x_sb[0][:], x_rows[0]).then_inc(x_loaded[0], 16)
            for w, wt in ((LEFT, wt_left), (RIGHT, wt_right), (SELF, wt_self)):
                sp.dma_start(w_raw[w][:], wt.rearrange("(c p) e -> p c e", p=P)).then_inc(w_loaded[w], 16)
                if w == LEFT:
                    sp.dma_start(adj_sb[0][:], adj_rows[0]).then_inc(adj_loaded[0], 16)
            for to, vector in ((bias[LEFT], b_left), (bias[RIGHT], b_right), (bias[SELF], b_self),
                               (gamma_sb, gamma), (beta_sb, beta)):
                sp.dma_start(to[:], vector.partition_broadcast(P)).then_inc(vectors_loaded, 16)
            for b in range(1, UNROLL - 1):
                load(b, b)

            def store(at, slot):
                sp.wait_ge(out_ready, at.n(T, 0))
                sp.dma_start(out_rows[at.n(1, -1)], out_sb[slot][:]).then_inc(stored[slot], 16)

            def one(at):
                if at.b != 0:
                    sp.wait_ge(y_ready, at.n(T, 0))
                if not at.fixed or at.b + UNROLL - 1 <= LAST:
                    load(at.n(1, UNROLL - 1), (at.u - 1) % UNROLL)
                if at.b != 0:
                    store(at, (at.u - 1) % 2)

            every_batch(sp, BATCHES, one)
            store(Batch(BATCHES // UNROLL, 0), LAST % 2)
            for s in stored:
                sp.wait_ge(s, 16 * (BATCHES // 2))

        @block.tensor
        def _(pe):
            def turn(at, t):
                if t == 0:
                    pe.wait_ge(x_loaded[at.u], at.uses(UNROLL, 1))
                if at.b != 0 or t:
                    pe.wait_ge(xt_lo_ready, at.n(T, t))
                for c in range(C):
                    mm = nc.tensor.transpose(ps_turn[:, c, :], x_sb[at.u][:, t, c * P:(c + 1) * P], ident[:])
                mm.then_inc(turned, 1)

            def product(to, pairs):
                passes = [(s[i], m[j]) for s, m in pairs for i, j in ((0, 0), (0, 1), (1, 0))]
                for k, (stationary, moving) in enumerate(passes):
                    mm = nc.tensor.matmul(to, stationary, moving, start=(k == 0), stop=(k == len(passes) - 1))
                return mm

            def xt(at, c, a, b):
                par = at.u % 2
                return xt_hi[par][:, c, a:b], xt_lo[par][:, c, a:b]

            def scores(at):
                pe.wait_ge(xt_lo_ready, at.n(T, T))
                if at.b != 0:
                    pe.wait_ge(exp_ready, at.n(T, 0))
                for t in range(T):
                    mm = product(ps_scores[:, t, :], [(xt(at, c, t * P, (t + 1) * P), xt(at, c, 0, L)) for c in range(C)])
                mm.then_inc(scores_ready, 1)

            def project(at, g):
                w, t = GROUPS[g]
                if at.b == 0 and t == 0:
                    pe.wait_ge(w_lo_ready, w + 1)
                if at.b != 0 or g >= PBANKS:
                    pe.wait_ge(proj_biased, at.n(NG, g + 1 - PBANKS))
                product(ps_proj[g % PBANKS][:, 0:H],
                        [(xt(at, c, t * P, (t + 1) * P), (w_hi[w][:, c, :], w_lo[w][:, c, :])) for c in range(C)]
                        ).then_inc(proj_ready, 1)

            def turn_delta(at):
                pe.wait_ge(delta_ready, at.n(T, T))
                if at.b != 0:
                    pe.wait_ge(dt_lo_ready, at.n(1, 0))
                for i, (m, t) in enumerate(BLOCKS):
                    mm = nc.tensor.transpose(ps_dt[:, i, :], delta[:, t, m * P:(m + 1) * P], ident[:])
                mm.then_inc(dt_ready, 1)

            def attend(at, t):
                if t == 0:
                    pe.wait_ge(triangles_ready, at.n(2, 2))
                if at.b != 0:
                    pe.wait_ge(context_ready, at.n(T, t + 1 - T))
                from_ = (dt_full, dt_left, dt_right)
                mm = None
                for k, (which, blk, g) in enumerate(ATTEND[t]):
                    pe.wait_ge(proj_lo_ready, at.n(NSPLIT, g + 1))
                    hi, lo = (from_[which][:, half, blk, :] for half in range(2))
                    m_hi, m_lo = proj_hi[:, g, :], proj_lo[:, g, :]
                    for j, (s, m) in enumerate(((hi, m_hi), (hi, m_lo), (lo, m_hi))):
                        mm = nc.tensor.matmul(ps_ctx[t][:, 0:H], s, m, start=(k == 0 and j == 0), stop=(k == 2 and j == 2))
                mm.then_inc(ctx_ready, 1)

            pe.wait_ge(ident_ready, 1)
            first = Batch(0, 0)
            turn(first, 0)
            turn(first, 1)
            scores(first)

            def one(at):
                nxt = Batch(at.turn, at.u + 1) if at.u + 1 < UNROLL else Batch(at.turn + 1, 0)
                has_next = at.b != LAST
                project(at, 0)
                project(at, 1)
                turn_delta(at)
                project(at, 2)
                project(at, 3)
                if has_next:
                    turn(nxt, 0)
                project(at, 4)
                if has_next:
                    turn(nxt, 1)
                project(at, 5)
                if has_next:
                    scores(nxt)
                for t in range(T):
                    attend(at, t)

            every_batch(pe, BATCHES, one)

        @block.scalar
        def _(act):
            def split_xt(at, t):
                act.wait_ge(turned, at.n(T, t + 1))
                nc.scalar.activation(xt_hi[at.u % 2][:, :, t * P:(t + 1) * P], ps_turn[:], ACT.Copy).then_inc(xt_hi_ready, 1)

            def exps(at):
                act.wait_ge(neg_max_ready, at.n(1, 1))
                for t in range(T):
                    nc.scalar.activation(e_sb[:, t, :], ps_scores[:, t, :], ACT.Exp, bias=neg_max[:, t:t + 1],
                                         scale=SCALE, accum_out=z_sum[:, t:t + 1]).then_inc(exp_ready, 1)

            def split_proj(at, g):
                act.wait_ge(proj_biased, at.n(NG, g + 1))
                nc.scalar.activation(proj_hi[:, g, :], proj[:, g, :], ACT.Copy).then_inc(proj_hi_ready, 1)

            def split_delta(at):
                act.wait_ge(dt_ready, at.n(1, 1))
                nc.scalar.activation(dt_full[:, 0, :, :], ps_dt[:], ACT.Copy).then_inc(dt_hi_ready, 1)

            def normalise(at):
                act.wait_ge(shift1_ready, at.n(1, 0))
                for t in range(T):
                    nc.scalar.activation(normed[:, t, :], context[:, t, :], ACT.Identity, bias=shift1[:, t:t + 1],
                                         scale=scale1[:, t:t + 1]).then_inc(normed_ready, 1)

            def outputs(at, slot):
                act.wait_ge(shift2_ready, at.n(1, 0))
                if not at.fixed or at.b >= 3:
                    j = Batch(at.turn, at.u - 3) if at.u >= 3 else Batch(at.turn - 1, at.u + 1)
                    act.wait_ge(stored[slot], j.uses(2, 1))
                for t in range(T):
                    nc.scalar.activation(out_sb[slot][:, t, :], y_sb[:, t, :], ACT.Identity, bias=shift2[:, t:t + 1],
                                         scale=scale2[:, t:t + 1]).then_inc(out_ready, 1)

            first = Batch(0, 0)
            split_xt(first, 0)
            split_xt(first, 1)
            for w in range(3):
                act.wait_ge(w_loaded[w], 16)
                nc.scalar.activation(w_hi[w][:], w_raw[w][:], ACT.Copy).then_inc(w_hi_ready, 1)
                if w == 0:
                    exps(first)

            def one(at):
                nxt = Batch(at.turn, at.u + 1) if at.u + 1 < UNROLL else Batch(at.turn + 1, 0)
                has_next = at.b != LAST
                split_proj(at, 0)
                if at.b != 0:
                    normalise(at)
                split_proj(at, 1)
                split_delta(at)
                split_proj(at, 2)
                split_proj(at, 3)
                if has_next:
                    split_xt(nxt, 0)
                    split_xt(nxt, 1)
                    exps(nxt)
                if at.b != 0:
                    outputs(at, (at.u - 1) % 2)

            every_batch(act, BATCHES, one)
            end = Batch(BATCHES // UNROLL, 0)
            normalise(end)
            outputs(end, LAST % 2)

        @block.vector
        def _(dve):
            def split_xt(at, t):
                par, cols = at.u % 2, slice(t * P, (t + 1) * P)
                dve.wait_ge(xt_hi_ready, at.n(T, t + 1))
                nc.vector.tensor_tensor(xt_lo[par][:, :, cols], ps_turn[:], xt_hi[par][:, :, cols].bitcast(F32),
                                        ALU.subtract).then_inc(xt_lo_ready, 1)

            def maxima(at):
                dve.wait_ge(scores_ready, at.n(1, 1))
                nc.vector.reduce_max(row_max[:], ps_scores[:], AX).then_inc(row_max_ready, 1)

            def negate_maxima(at):
                dve.wait_ge(row_max_ready, at.n(1, 1))
                nc.vector.tensor_scalar(neg_max[:], row_max[:], -SCALE, None, ALU.mult).then_inc(neg_max_ready, 1)

            def deltas(at):
                par = at.u % 2
                dve.wait_ge(adj_loaded[at.u], at.uses(UNROLL, 1))
                for t in range(T):
                    dve.wait_ge(exp_ready, at.n(T, t + 1))
                    nc.vector.tensor_tensor_reduce(delta[:, t, :], e_sb[:, t, :], adj_sb[at.u][:, t, :], 1.0, 0.0,
                                                   ALU.mult, ALU.add, s_sum[:, t:t + 1]).then_inc(delta_ready, 1)
                dve.wait_ge(delta_ready, at.n(T, T))
                nc.vector.scalar_tensor_tensor(denom[:], z_sum[:], SUM_EPS, s_sum[:], ALU.mult, ALU.add
                                               ).then_inc(denom_ready, 1)
                for t in range(T):
                    nc.vector.scalar_tensor_tensor(on_diag[:, t, :], delta[:, t, t * P:(t + 1) * P], 1.0, ident[:],
                                                   ALU.mult, ALU.mult, accum_out=diag[par][:, t:t + 1]
                                                   ).then_inc(softmax_done, 1)
                dve.wait_ge(denom_ready, at.n(1, 1))
                nc.vector.reciprocal(recip[par][:], denom[:]).then_inc(softmax_done, 1)

            def add_bias(at, g):
                w, t = GROUPS[g]
                to = proj[:, g, :] if g < NSPLIT else proj_self[:, t, :]
                dve.wait_ge(proj_ready, at.n(NG, g + 1))
                if at.b != 0 and g < NSPLIT:
                    dve.wait_ge(proj_lo_ready, at.n(NSPLIT, g + 1 - NSPLIT))
                nc.vector.tensor_tensor(to, ps_proj[g % PBANKS][:, 0:H], bias[w][:], ALU.add).then_inc(proj_biased, 1)

            def split_delta(at):
                dve.wait_ge(dt_hi_ready, at.n(1, 1))
                nc.vector.tensor_tensor(dt_full[:, 1, :, :], ps_dt[:], dt_full[:, 0, :, :].bitcast(F32),
                                        ALU.subtract).then_inc(dt_lo_ready, 1)

            def contexts(at, par):
                dve.wait_ge(softmax_done, at.n(3, 0))
                dve.wait_ge(proj_biased, at.n(NG, 0))
                for t in range(T):
                    dve.wait_ge(ctx_ready, at.n(T, t + 1 - T))
                    nc.vector.scalar_tensor_tensor(context[:, t, :], proj_self[:, t, :], diag[par][:, t:t + 1],
                                                   ps_ctx[t][:, 0:H], ALU.mult, ALU.add).then_inc(context_ready, 1)
                    dve.wait_ge(context_ready, at.n(T, t + 1 - T))
                    nc.vector.bn_stats(stats1[:, t, :], context[:, t, :]).then_inc(stats1_ready, 1)
                dve.wait_ge(stats1_ready, at.n(T, 0))
                nc.vector.tensor_tensor(recip_sq[:], recip[par][:], recip[par][:], ALU.mult).then_inc(recip_sq_ready, 1)
                for t in range(T):
                    nc.vector.bn_aggr(mv1[:, t, :], stats1[:, t, :]).then_inc(mv1_ready, 1)
                dve.wait_ge(recip_sq_ready, at.n(1, 0))
                dve.wait_ge(mv1_ready, at.n(T, 0))
                nc.vector.tensor_tensor(var1[:], mv1[:, :, 1], recip_sq[:], ALU.mult).then_inc(var1_ready, 1)
                dve.wait_ge(var1_ready, at.n(1, 0))
                nc.vector.tensor_scalar(var1_eps[:], var1[:], LN1_EPS, None, ALU.add).then_inc(var1_eps_ready, 1)

            def norm1(at, par):
                dve.wait_ge(pow1_ready, at.n(1, 0))
                nc.vector.tensor_tensor(scale1[:], pow1[:], recip[par][:], ALU.mult).then_inc(scale1_ready, 1)
                dve.wait_ge(scale1_ready, at.n(1, 0))
                nc.vector.scalar_tensor_tensor(shift1[:], mv1[:, :, 0], -1.0, scale1[:], ALU.mult, ALU.mult
                                               ).then_inc(shift1_ready, 1)

            def residual(at, t, slot):
                dve.wait_ge(shifted_ready, at.n(T, t + 1 - T))
                nc.vector.scalar_tensor_tensor(y_sb[:, t, :], shifted[:, t, :], 0.0, x_sb[slot][:, t, :],
                                               ALU.max, ALU.add).then_inc(y_ready, 1)
                dve.wait_ge(y_ready, at.n(T, t + 1 - T))
                nc.vector.bn_stats(stats2[:, t, :], y_sb[:, t, :]).then_inc(stats2_ready, 1)

            def norm2_variance(at):
                for t in range(T):
                    nc.vector.bn_aggr(mv2[:, t, :], stats2[:, t, :]).then_inc(mv2_ready, 1)
                dve.wait_ge(mv2_ready, at.n(T, 0))
                nc.vector.tensor_scalar(var2_eps[:], mv2[:, :, 1], LN2_EPS, None, ALU.add).then_inc(var2_eps_ready, 1)

            def norm2(at):
                dve.wait_ge(scale2_ready, at.n(1, 0))
                nc.vector.scalar_tensor_tensor(shift2[:], mv2[:, :, 0], -1.0, scale2[:], ALU.mult, ALU.mult
                                               ).then_inc(shift2_ready, 1)

            def split_weight(w):
                dve.wait_ge(w_hi_ready, w + 1)
                nc.vector.tensor_tensor(w_lo[w][:], w_raw[w][:], w_hi[w][:].bitcast(F32), ALU.subtract
                                        ).then_inc(w_lo_ready, 1)

            first = Batch(0, 0)
            dve.wait_ge(ident_ready, 1)
            split_xt(first, 0)
            split_xt(first, 1)
            split_weight(0)
            maxima(first)
            negate_maxima(first)
            deltas(first)
            split_weight(1)
            split_weight(2)
            dve.wait_ge(vectors_loaded, 5 * 16)

            def one(at):
                nxt = Batch(at.turn, at.u + 1) if at.u + 1 < UNROLL else Batch(at.turn + 1, 0)
                has_next, has_last = at.b != LAST, at.b != 0
                par, slot = (at.u - 1) % 2, (at.u - 1) % UNROLL
                if has_last:
                    contexts(at, par)
                add_bias(at, 0)
                if has_last:
                    norm1(at, par)
                add_bias(at, 1)
                split_delta(at)
                add_bias(at, 2)
                if has_last:
                    residual(at, 0, slot)
                add_bias(at, 3)
                if has_next:
                    split_xt(nxt, 0)
                add_bias(at, 4)
                if has_next:
                    split_xt(nxt, 1)
                add_bias(at, 5)
                if has_last:
                    residual(at, 1, slot)
                    dve.wait_ge(stats2_ready, at.n(T, 0))
                if has_next:
                    maxima(nxt)
                if has_last:
                    norm2_variance(at)
                if has_next:
                    negate_maxima(nxt)
                if has_last:
                    norm2(at)
                if has_next:
                    deltas(nxt)

            every_batch(dve, BATCHES, one)
            end = Batch(BATCHES // UNROLL, 0)
            par, slot = LAST % 2, LAST % UNROLL
            contexts(end, par)
            norm1(end, par)
            residual(end, 0, slot)
            residual(end, 1, slot)
            dve.wait_ge(stats2_ready, end.n(T, 0))
            norm2_variance(end)
            norm2(end)

        @block.gpsimd
        def _(pool):
            nc.gpsimd.memset(ident[:], 0.0).then_inc(ident_zeroed, 1)
            nc.gpsimd.memset(minus_half[:], -0.5).then_inc(minus_half_ready, 1)
            pool.wait_ge(ident_zeroed, 1)
            nc.gpsimd.affine_select(out=ident[:], in_=ident[:], compare_op=ALU.not_equal, fill=1.0, base=0,
                                    pattern=[[-1, P]], channel_multiplier=1).then_inc(ident_ready, 1)
            pool.wait_ge(minus_half_ready, 1)
            pool.wait_ge(vectors_loaded, 5 * 16)

            def split_proj(at, g):
                if g == 1:
                    pool.wait_ge(dt_lo_ready, at.n(1, 1))
                pool.wait_ge(proj_hi_ready, at.n(NSPLIT, g + 1))
                nc.gpsimd.tensor_tensor(proj_lo[:, g, :], proj[:, g, :], proj_hi[:, g, :].bitcast(F32), ALU.subtract
                                        ).then_inc(proj_lo_ready, 1)

            def triangles(at):
                blocks = dt_full[:, :, 0:T, :].bitcast(F32).rearrange("p h t l -> p h (t l)")
                for to, sign in ((dt_left, 1), (dt_right, -1)):
                    nc.gpsimd.affine_select(out=to[:].rearrange("p h t l -> p h (t l)"), in_=blocks, compare_op=ALU.is_gt, fill=0.0, base=0,
                                            pattern=[[0, 2], [0, T], [-sign, P]], channel_multiplier=sign
                                            ).then_inc(triangles_ready, 1)

            def power1(at):
                pool.wait_ge(var1_eps_ready, at.n(1, 0))
                nc.gpsimd.tensor_tensor(pow1[:], var1_eps[:], minus_half[:], ALU.pow).then_inc(pow1_ready, 1)

            def affine(at, t):
                pool.wait_ge(normed_ready, at.n(T, t + 1 - T))
                nc.gpsimd.tensor_tensor(scaled[:, t, :], normed[:, t, :], gamma_sb[:], ALU.mult).then_inc(scaled_ready, 1)
                pool.wait_ge(scaled_ready, at.n(T, t + 1 - T))
                nc.gpsimd.tensor_tensor(shifted[:, t, :], scaled[:, t, :], beta_sb[:], ALU.add).then_inc(shifted_ready, 1)

            def power2(at):
                pool.wait_ge(var2_eps_ready, at.n(1, 0))
                nc.gpsimd.tensor_tensor(scale2[:], var2_eps[:], minus_half[:], ALU.pow).then_inc(scale2_ready, 1)

            def one(at):
                has_last = at.b != 0
                if has_last:
                    power1(at)
                split_proj(at, 0)
                if has_last:
                    affine(at, 0)
                split_proj(at, 1)
                triangles(at)
                if has_last:
                    affine(at, 1)
                split_proj(at, 2)
                split_proj(at, 3)
                if has_last:
                    power2(at)

            every_batch(pool, BATCHES, one)
            end = Batch(BATCHES // UNROLL, 0)
            power1(end)
            affine(end, 0)
            affine(end, 1)
            power2(end)


_INS = ["x", "adj", "L0_gnn_W_left", "L0_gnn_b_left", "L0_gnn_W_self", "L0_gnn_b_self", "L0_gnn_W_right",
        "L0_gnn_b_right", "L0_gnn_gamma", "L0_gnn_beta"]


def kernel(**inputs):
    import numpy as _np
    import concourse.bacc as _bacc
    from concourse import mybir as _mybir
    from concourse.bass_utils import run_bass_kernel_spmd as _run

    nc = _bacc.Bacc("TRN2", target_bir_lowering=False, num_devices=1)
    arrays, args = {}, []
    for name in _INS:
        a = _np.asarray(inputs[name])
        a = _np.ascontiguousarray(a.T if "_W_" in name else a)
        arrays[f"in_{name}"] = a
        args.append(nc.dram_tensor(f"in_{name}", a.shape, _mybir.dt.from_np(a.dtype), kind="ExternalInput").ap())
    shape = arrays["in_x"].shape
    out = nc.dram_tensor("out_dram", shape, _mybir.dt.float32, kind="ExternalOutput").ap()
    gnn_resnorm(nc, *args, out)
    r = _run(nc, [arrays], core_ids=[0])
    return r.results[0]["out_dram"]
```

```python
from contextlib import ExitStack

import concourse.bass as bass
from concourse import mybir

P = 128
UNROLL = 4
F32 = mybir.dt.float32
F32R = mybir.dt.float32r
ALU = mybir.AluOpType
ACT = mybir.ActivationFunctionType
AX = mybir.AxisListType.X
LN1_EPS = 1e-12
LN2_EPS = 1e-5
SUM_EPS = 1e-10


class Batch:

    def __init__(self, turn, u):
        self.turn, self.u = turn, u
        self.b = UNROLL * turn + u if isinstance(turn, int) else None

    def plus(self, d):
        return Batch(self.turn, self.u + d)

    def exists(self, batches):
        return self.b is None or 0 <= self.b < batches

    def n(self, per, c=0):
        return self.turn * (UNROLL * per) + (self.u * per + c)

    def slot(self, ring):
        return self.u % ring

    def loads(self, ring, c=0):
        return self.turn * (16 * UNROLL // ring) + 16 * (self.u // ring + c)


def every_batch(eng, batches, one):
    turns = batches // UNROLL
    for u in range(UNROLL):
        one(Batch(0, u))
    with eng.Fori(1, turns - 1) as turn:
        for u in range(UNROLL):
            one(Batch(turn, u))
    for u in range(UNROLL):
        one(Batch(turns - 1, u))


def gnn_resnorm(nc, x, x_t, adj, wt_left, b_left, wt_self, b_self, wt_right, b_right, gamma, beta, out):
    BATCHES, L, H = x.shape
    T = L // P
    C = H // P
    assert T == 2 and C == 3 and BATCHES % UNROLL == 0
    SCALE = 1.0 / float(H) ** 0.5
    LEFT, RIGHT, SELF = range(3)
    WARM_UP = 20
    GROUPS = [(LEFT, 0), (RIGHT, 0), (LEFT, 1), (RIGHT, 1), (SELF, 0), (SELF, 1)]
    NG, NSPLIT, PBANKS = 6, 4, 4
    BLOCKS = [(0, 0), (1, 1), (1, 0), (0, 1)]
    FULL, MASK_LEFT, MASK_RIGHT = range(3)
    ATTEND = [
        [(MASK_LEFT, 0, 0), (MASK_RIGHT, 0, 1), (FULL, 2, 2)],
        [(FULL, 3, 1), (MASK_LEFT, 1, 2), (MASK_RIGHT, 1, 3)],
    ]

    with ExitStack() as ctx:
        def sb(name, shape, dt=F32):
            return ctx.enter_context(nc.sbuf_tensor(name, shape, dt))

        def psum(name, shape):
            return ctx.enter_context(nc.psum_tensor(name, shape, F32))

        def sem(name):
            return ctx.enter_context(nc.semaphore(name))

        ident = sb("ident", [P, P])
        minus_half = sb("minus_half", [P, T])
        w_raw = [sb(f"w_raw{w}", [P, C, H]) for w in range(3)]
        w_hi = [sb(f"w_hi{w}", [P, C, H], F32R) for w in range(3)]
        w_lo = [sb(f"w_lo{w}", [P, C, H], F32R) for w in range(3)]
        bias = [sb(f"bias{w}", [P, H]) for w in range(3)]
        gamma_sb = sb("gamma_sb", [P, H])
        beta_sb = sb("beta_sb", [P, H])
        x_sb = [sb(f"x_sb{i}", [P, T, H]) for i in range(UNROLL)]
        xt_sb = [sb(f"xt_sb{i}", [P, C, L]) for i in range(UNROLL)]
        adj_sb = [sb(f"adj_sb{i}", [P, T, L]) for i in range(UNROLL)]
        xt_hi = [sb(f"xt_hi{i}", [P, C, L], F32R) for i in range(2)]
        xt_lo = [sb(f"xt_lo{i}", [P, C, L], F32R) for i in range(2)]
        diag = [sb(f"diag{i}", [P, T]) for i in range(2)]
        recip = [sb(f"recip{i}", [P, T]) for i in range(2)]
        out_sb = [sb(f"out_sb{i}", [P, T, H]) for i in range(2)]
        row_max = sb("row_max", [P, T])
        neg_max = sb("neg_max", [P, T])
        z_sum = sb("z_sum", [P, T])
        e_sb = sb("e_sb", [P, T, L])
        delta = sb("delta", [P, T, L])
        s_sum = sb("s_sum", [P, T])
        denom = sb("denom", [P, T])
        on_diag = sb("on_diag", [P, T, P])
        dt_full = sb("dt_full", [P, 2, T * T, P], F32R)
        dt_left = sb("dt_left", [P, 2, T, P], F32R)
        dt_right = sb("dt_right", [P, 2, T, P], F32R)
        proj = sb("proj", [P, NSPLIT, H])
        proj_hi = sb("proj_hi", [P, NSPLIT, H], F32R)
        proj_lo = sb("proj_lo", [P, NSPLIT, H], F32R)
        proj_self = sb("proj_self", [P, T, H])
        context = sb("context", [P, T, H])
        stats1 = sb("stats1", [P, T, 6])
        mv1 = sb("mv1", [P, T, 2])
        recip_sq = sb("recip_sq", [P, T])
        var1_eps = sb("var1_eps", [P, T])
        pow1 = sb("pow1", [P, T])
        scale1 = sb("scale1", [P, T])
        shift1 = sb("shift1", [P, T])
        normed = sb("normed", [P, T, H])
        scaled = sb("scaled", [P, T, H])
        shifted = sb("shifted", [P, T, H])
        y_sb = sb("y_sb", [P, T, H])
        stats2 = sb("stats2", [P, T, 6])
        mv2 = sb("mv2", [P, T, 2])
        var2_eps = sb("var2_eps", [P, T])
        scale2 = sb("scale2", [P, T])
        shift2 = sb("shift2", [P, T])
        ps_scores = psum("ps_scores", [P, T, L])
        ps_dt = psum("ps_dt", [P, T * T, P])
        ps_proj = [psum(f"ps_proj{i}", [P, 512]) for i in range(PBANKS)]
        ps_ctx = [psum(f"ps_ctx{i}", [P, 512]) for i in range(T)]

        x_loaded = [sem(f"x_loaded{i}") for i in range(UNROLL)]
        xt_loaded = [sem(f"xt_loaded{i}") for i in range(UNROLL)]
        adj_loaded = [sem(f"adj_loaded{i}") for i in range(UNROLL)]
        w_loaded = [sem(f"w_loaded{w}") for w in range(3)]
        vectors_loaded = sem("vectors_loaded")
        stored = [sem(f"stored{i}") for i in range(2)]
        ident_zeroed = sem("ident_zeroed")
        ident_ready = sem("ident_ready")
        minus_half_ready = sem("minus_half_ready")
        w_hi_ready = sem("w_hi_ready")
        w_lo_ready = [sem(f"w_lo_ready{w}") for w in range(3)]
        scores_ready = sem("scores_ready")
        dt_ready = sem("dt_ready")
        proj_ready = sem("proj_ready")
        ctx_ready = sem("ctx_ready")
        xt_hi_ready = sem("xt_hi_ready")
        exp_ready = sem("exp_ready")
        dt_hi_ready = sem("dt_hi_ready")
        proj_hi_ready = sem("proj_hi_ready")
        normed_ready = sem("normed_ready")
        out_ready = sem("out_ready")
        xt_lo_ready = sem("xt_lo_ready")
        row_max_ready = sem("row_max_ready")
        neg_max_ready = sem("neg_max_ready")
        delta_ready = sem("delta_ready")
        denom_ready = sem("denom_ready")
        softmax_done = sem("softmax_done")
        dt_lo_ready = sem("dt_lo_ready")
        proj_biased = sem("proj_biased")
        context_ready = sem("context_ready")
        stats1_ready = sem("stats1_ready")
        mv1_ready = sem("mv1_ready")
        recip_sq_ready = sem("recip_sq_ready")
        var1_eps_ready = sem("var1_eps_ready")
        scale1_ready = sem("scale1_ready")
        shift1_ready = sem("shift1_ready")
        y_ready = sem("y_ready")
        stats2_ready = sem("stats2_ready")
        mv2_ready = sem("mv2_ready")
        var2_eps_ready = sem("var2_eps_ready")
        shift2_ready = sem("shift2_ready")
        proj_lo_ready = sem("proj_lo_ready")
        triangles_ready = sem("triangles_ready")
        pow1_ready = sem("pow1_ready")
        scaled_ready = [sem(f"scaled_ready{t}") for t in range(T)]
        shifted_ready = [sem(f"shifted_ready{t}") for t in range(T)]
        scale2_ready = sem("scale2_ready")

        x_rows = x.rearrange("b (t p) h -> b p t h", p=P)
        xt_rows = x_t.rearrange("b (c p) l -> b p c l", p=P)
        adj_rows = adj.rearrange("b (t p) m -> b p t m", p=P)
        out_rows = out.rearrange("b (t p) h -> b p t h", p=P)

        def bank(at, g):
            assert UNROLL * NG % PBANKS == 0
            return (at.u * NG + g) % PBANKS

        def affine(eng, ops, at, t):
            eng.wait_ge(normed_ready, at.n(T, t + 1))
            ops.tensor_tensor(scaled[:, t, :], normed[:, t, :], gamma_sb[:], ALU.mult).then_inc(scaled_ready[t], 1)
            eng.wait_ge(scaled_ready[t], at.n(1, 1))
            ops.tensor_tensor(shifted[:, t, :], scaled[:, t, :], beta_sb[:], ALU.add).then_inc(shifted_ready[t], 1)

        block = ctx.enter_context(nc.Block())

        @block.sync
        def _(sp):
            def load(b, slot):
                sp.dma_start(xt_sb[slot][:], xt_rows[b]).then_inc(xt_loaded[slot], 16)
                sp.dma_start(x_sb[slot][:], x_rows[b]).then_inc(x_loaded[slot], 16)
                sp.dma_start(adj_sb[slot][:], adj_rows[b]).then_inc(adj_loaded[slot], 16)

            sp.dma_start(xt_sb[0][:], xt_rows[0]).then_inc(xt_loaded[0], 16)
            for w, wt in ((LEFT, wt_left), (RIGHT, wt_right), (SELF, wt_self)):
                sp.dma_start(w_raw[w][:], wt.rearrange("(c p) e -> p c e", p=P)).then_inc(w_loaded[w], 16)
                if w == LEFT:
                    sp.dma_start(adj_sb[0][:], adj_rows[0]).then_inc(adj_loaded[0], 16)
            for to, vector in ((bias[LEFT], b_left), (bias[RIGHT], b_right), (bias[SELF], b_self),
                               (gamma_sb, gamma), (beta_sb, beta)):
                sp.dma_start(to[:], vector.partition_broadcast(P)).then_inc(vectors_loaded, 16)
            sp.dma_start(x_sb[0][:], x_rows[0]).then_inc(x_loaded[0], 16)
            for b in range(1, UNROLL):
                load(b, b)

            def store(at):
                sp.wait_ge(out_ready, at.n(T, T))
                sp.dma_start(out_rows[at.n(1)], out_sb[at.slot(2)][:]).then_inc(stored[at.slot(2)], 16)

            def one(at):
                ahead, behind = at.plus(2), at.plus(-2)
                if behind.exists(BATCHES):
                    if ahead.exists(BATCHES):
                        sp.wait_ge(y_ready, behind.n(T, T))
                        load(ahead.n(1), ahead.slot(UNROLL))
                    store(behind)

            every_batch(sp, BATCHES, one)
            end = Batch(BATCHES // UNROLL, 0)
            store(end.plus(-2))
            store(end.plus(-1))
            for s in stored:
                sp.wait_ge(s, 16 * (BATCHES // 2))

        @block.tensor
        def _(pe):
            def product(to, pairs):
                passes = [(s[i], m[j]) for s, m in pairs for i, j in ((0, 0), (0, 1), (1, 0))]
                for k, (stationary, moving) in enumerate(passes):
                    mm = nc.tensor.matmul(to, stationary, moving, start=(k == 0), stop=(k == len(passes) - 1))
                return mm

            def xt(at, c, a, b):
                par = at.slot(2)
                return xt_hi[par][:, c, a:b], xt_lo[par][:, c, a:b]

            def scores(at):
                pe.wait_ge(xt_lo_ready, at.n(1, 1))
                if at.b != 0:
                    pe.wait_ge(exp_ready, at.n(T, 0))
                for t in range(T):
                    mm = product(ps_scores[:, t, :], [(xt(at, c, t * P, (t + 1) * P), xt(at, c, 0, L)) for c in range(C)])
                mm.then_inc(scores_ready, 1)

            def project(at, g):
                w, t = GROUPS[g]
                if at.b == 0 and t == 0:
                    pe.wait_ge(w_lo_ready[w], 1)
                if at.b != 0 or g >= PBANKS:
                    pe.wait_ge(proj_biased, at.n(NG, g + 1 - PBANKS))
                product(ps_proj[bank(at, g)][:, 0:H],
                        [(xt(at, c, t * P, (t + 1) * P), (w_hi[w][:, c, :], w_lo[w][:, c, :])) for c in range(C)]
                        ).then_inc(proj_ready, 1)

            def turn_delta(at):
                pe.wait_ge(delta_ready, at.n(T, T))
                if at.b != 0:
                    pe.wait_ge(dt_lo_ready, at.n(1, 0))
                for i, (m, t) in enumerate(BLOCKS):
                    mm = nc.tensor.transpose(ps_dt[:, i, :], delta[:, t, m * P:(m + 1) * P], ident[:])
                mm.then_inc(dt_ready, 1)

            def attend(at, t):
                if t == 0:
                    pe.wait_ge(triangles_ready, at.n(2, 2))
                if at.b != 0:
                    pe.wait_ge(context_ready, at.n(T, t + 1 - T))
                from_ = (dt_full, dt_left, dt_right)
                mm = None
                for k, (which, blk, g) in enumerate(ATTEND[t]):
                    pe.wait_ge(proj_lo_ready, at.n(NSPLIT, g + 1))
                    hi, lo = (from_[which][:, half, blk, :] for half in range(2))
                    m_hi, m_lo = proj_hi[:, g, :], proj_lo[:, g, :]
                    for j, (s, m) in enumerate(((hi, m_hi), (hi, m_lo), (lo, m_hi))):
                        mm = nc.tensor.matmul(ps_ctx[t][:, 0:H], s, m, start=(k == 0 and j == 0), stop=(k == 2 and j == 2))
                mm.then_inc(ctx_ready, 1)

            pe.wait_ge(ident_ready, 1)
            for _ in range(WARM_UP):
                nc.tensor.transpose(ps_dt[:, 0, :], ident[:], ident[:])
            first = Batch(0, 0)
            scores(first)

            def one(at):
                nxt = at.plus(1)
                project(at, 0)
                project(at, 1)
                turn_delta(at)
                project(at, 2)
                project(at, 3)
                project(at, 4)
                project(at, 5)
                if nxt.exists(BATCHES):
                    scores(nxt)
                for t in range(T):
                    attend(at, t)

            every_batch(pe, BATCHES, one)

        @block.scalar
        def _(act):
            def split_xt(at):
                act.wait_ge(xt_loaded[at.slot(UNROLL)], at.loads(UNROLL, 1))
                nc.scalar.activation(xt_hi[at.slot(2)][:], xt_sb[at.slot(UNROLL)][:], ACT.Copy).then_inc(xt_hi_ready, 1)

            def exps(at):
                act.wait_ge(neg_max_ready, at.n(1, 1))
                for t in range(T):
                    nc.scalar.activation(e_sb[:, t, :], ps_scores[:, t, :], ACT.Exp, bias=neg_max[:, t:t + 1],
                                         scale=SCALE, accum_out=z_sum[:, t:t + 1]).then_inc(exp_ready, 1)

            def split_proj(at, g):
                act.wait_ge(proj_biased, at.n(NG, g + 1))
                nc.scalar.activation(proj_hi[:, g, :], proj[:, g, :], ACT.Copy).then_inc(proj_hi_ready, 1)

            def split_delta(at):
                act.wait_ge(dt_ready, at.n(1, 1))
                nc.scalar.activation(dt_full[:, 0, :, :], ps_dt[:], ACT.Copy).then_inc(dt_hi_ready, 1)

            def normalise(at):
                act.wait_ge(shift1_ready, at.n(1, 1))
                for t in range(T):
                    nc.scalar.activation(normed[:, t, :], context[:, t, :], ACT.Identity, bias=shift1[:, t:t + 1],
                                         scale=scale1[:, t:t + 1]).then_inc(normed_ready, 1)

            def outputs(at):
                act.wait_ge(shift2_ready, at.n(1, 1))
                if at.plus(-2).exists(BATCHES):
                    act.wait_ge(stored[at.slot(2)], at.loads(2, 0))
                for t in range(T):
                    nc.scalar.activation(out_sb[at.slot(2)][:, t, :], y_sb[:, t, :], ACT.Identity,
                                         bias=shift2[:, t:t + 1], scale=scale2[:, t:t + 1]).then_inc(out_ready, 1)

            first = Batch(0, 0)
            split_xt(first)
            for w in range(3):
                act.wait_ge(w_loaded[w], 16)
                nc.scalar.activation(w_hi[w][:], w_raw[w][:], ACT.Copy).then_inc(w_hi_ready, 1)
            exps(first)

            def one(at):
                nxt = at.plus(1)
                before, second = at.plus(-1), at.plus(-2)
                split_proj(at, 0)
                split_delta(at)
                split_proj(at, 1)
                if before.exists(BATCHES):
                    normalise(before)
                if nxt.exists(BATCHES):
                    split_xt(nxt)
                split_proj(at, 2)
                split_proj(at, 3)
                if second.exists(BATCHES):
                    outputs(second)
                if nxt.exists(BATCHES):
                    exps(nxt)

            every_batch(act, BATCHES, one)
            end = Batch(BATCHES // UNROLL, 0)
            normalise(end.plus(-1))
            outputs(end.plus(-2))
            outputs(end.plus(-1))

        @block.vector
        def _(dve):
            def split_xt(at):
                dve.wait_ge(xt_hi_ready, at.n(1, 1))
                nc.vector.tensor_tensor(xt_lo[at.slot(2)][:], xt_sb[at.slot(UNROLL)][:],
                                        xt_hi[at.slot(2)][:].bitcast(F32), ALU.subtract).then_inc(xt_lo_ready, 1)

            def maxima(at):
                dve.wait_ge(scores_ready, at.n(1, 1))
                nc.vector.reduce_max(row_max[:], ps_scores[:], AX).then_inc(row_max_ready, 1)

            def negate_maxima(at):
                dve.wait_ge(row_max_ready, at.n(1, 1))
                nc.vector.tensor_scalar(neg_max[:], row_max[:], -SCALE, None, ALU.mult).then_inc(neg_max_ready, 1)

            def deltas(at, t):
                if t == 0:
                    dve.wait_ge(adj_loaded[at.slot(UNROLL)], at.loads(UNROLL, 1))
                dve.wait_ge(exp_ready, at.n(T, t + 1))
                nc.vector.tensor_tensor_reduce(delta[:, t, :], e_sb[:, t, :], adj_sb[at.slot(UNROLL)][:, t, :], 1.0, 0.0,
                                               ALU.mult, ALU.add, s_sum[:, t:t + 1]).then_inc(delta_ready, 1)

            def softmax_end(at):
                par = at.slot(2)
                dve.wait_ge(delta_ready, at.n(T, T))
                nc.vector.scalar_tensor_tensor(denom[:], z_sum[:], SUM_EPS, s_sum[:], ALU.mult, ALU.add
                                               ).then_inc(denom_ready, 1)
                for t in range(T):
                    nc.vector.scalar_tensor_tensor(on_diag[:, t, :], delta[:, t, t * P:(t + 1) * P], 1.0, ident[:],
                                                   ALU.mult, ALU.mult, accum_out=diag[par][:, t:t + 1]
                                                   ).then_inc(softmax_done, 1)
                dve.wait_ge(denom_ready, at.n(1, 1))
                nc.vector.reciprocal(recip[par][:], denom[:]).then_inc(softmax_done, 1)

            def add_bias(at, g):
                w, t = GROUPS[g]
                to = proj[:, g, :] if g < NSPLIT else proj_self[:, t, :]
                dve.wait_ge(proj_ready, at.n(NG, g + 1))
                if at.b != 0 and g < NSPLIT:
                    dve.wait_ge(proj_lo_ready, at.n(NSPLIT, g + 1 - NSPLIT))
                nc.vector.tensor_tensor(to, ps_proj[bank(at, g)][:, 0:H], bias[w][:], ALU.add).then_inc(proj_biased, 1)

            def split_delta(at):
                dve.wait_ge(dt_hi_ready, at.n(1, 1))
                nc.vector.tensor_tensor(dt_full[:, 1, :, :], ps_dt[:], dt_full[:, 0, :, :].bitcast(F32),
                                        ALU.subtract).then_inc(dt_lo_ready, 1)

            def contexts(at, t):
                if t == 0:
                    dve.wait_ge(softmax_done, at.n(3, 3))
                    dve.wait_ge(proj_biased, at.n(NG, NG))
                dve.wait_ge(ctx_ready, at.n(T, t + 1))
                nc.vector.scalar_tensor_tensor(context[:, t, :], proj_self[:, t, :], diag[at.slot(2)][:, t:t + 1],
                                               ps_ctx[t][:, 0:H], ALU.mult, ALU.add).then_inc(context_ready, 1)

            def context_stats(at, t):
                dve.wait_ge(context_ready, at.n(T, t + 1))
                nc.vector.bn_stats(stats1[:, t, :], context[:, t, :]).then_inc(stats1_ready, 1)

            def norm1_variance(at):
                dve.wait_ge(stats1_ready, at.n(T, T))
                r = recip[at.slot(2)]
                nc.vector.tensor_tensor(recip_sq[:], r[:], r[:], ALU.mult).then_inc(recip_sq_ready, 1)
                for t in range(T):
                    nc.vector.bn_aggr(mv1[:, t, :], stats1[:, t, :]).then_inc(mv1_ready, 1)
                dve.wait_ge(recip_sq_ready, at.n(1, 1))
                for t in range(T):
                    dve.wait_ge(mv1_ready, at.n(T, t + 1))
                    nc.vector.tensor_scalar(var1_eps[:, t:t + 1], mv1[:, t, 1:2], recip_sq[:, t:t + 1], LN1_EPS,
                                            ALU.mult, ALU.add).then_inc(var1_eps_ready, 1)

            def norm1(at):
                dve.wait_ge(pow1_ready, at.n(1, 1))
                nc.vector.tensor_tensor(scale1[:], pow1[:], recip[at.slot(2)][:], ALU.mult).then_inc(scale1_ready, 1)
                dve.wait_ge(scale1_ready, at.n(1, 1))
                nc.vector.scalar_tensor_tensor(shift1[:], mv1[:, :, 0], -1.0, scale1[:], ALU.mult, ALU.mult
                                               ).then_inc(shift1_ready, 1)

            def residual(at, t):
                dve.wait_ge(shifted_ready[t], at.n(1, 1))
                if t == 0:
                    dve.wait_ge(x_loaded[at.slot(UNROLL)], at.loads(UNROLL, 1))
                if at.plus(-1).exists(BATCHES):
                    dve.wait_ge(out_ready, at.n(T, 0))
                nc.vector.scalar_tensor_tensor(y_sb[:, t, :], shifted[:, t, :], 0.0, x_sb[at.slot(UNROLL)][:, t, :],
                                               ALU.max, ALU.add).then_inc(y_ready, 1)

            def residual_stats(at, t):
                dve.wait_ge(y_ready, at.n(T, t + 1))
                nc.vector.bn_stats(stats2[:, t, :], y_sb[:, t, :]).then_inc(stats2_ready, 1)

            def norm2_variance(at):
                for t in range(T):
                    nc.vector.bn_aggr(mv2[:, t, :], stats2[:, t, :]).then_inc(mv2_ready, 1)
                dve.wait_ge(mv2_ready, at.n(T, T))
                nc.vector.tensor_scalar(var2_eps[:], mv2[:, :, 1], LN2_EPS, None, ALU.add).then_inc(var2_eps_ready, 1)

            def norm2(at):
                dve.wait_ge(scale2_ready, at.n(1, 1))
                nc.vector.scalar_tensor_tensor(shift2[:], mv2[:, :, 0], -1.0, scale2[:], ALU.mult, ALU.mult
                                               ).then_inc(shift2_ready, 1)

            def split_weight(w):
                dve.wait_ge(w_hi_ready, w + 1)
                nc.vector.tensor_tensor(w_lo[w][:], w_raw[w][:], w_hi[w][:].bitcast(F32), ALU.subtract
                                        ).then_inc(w_lo_ready[w], 1)

            first = Batch(0, 0)
            split_xt(first)
            split_weight(0)
            split_weight(1)
            maxima(first)
            negate_maxima(first)
            deltas(first, 0)
            deltas(first, 1)
            dve.wait_ge(ident_ready, 1)
            softmax_end(first)
            dve.wait_ge(vectors_loaded, 5 * 16)

            def one(at):
                before, second = at.plus(-1), at.plus(-2)
                nxt = at.plus(1)
                if before.exists(BATCHES):
                    norm1_variance(before)
                add_bias(at, 0)
                if before.exists(BATCHES):
                    softmax_end(at)
                    norm1(before)
                add_bias(at, 1)
                if second.exists(BATCHES):
                    residual(second, 1)
                split_delta(at)
                if second.exists(BATCHES):
                    residual_stats(second, 1)
                    dve.wait_ge(stats2_ready, second.n(T, T))
                add_bias(at, 2)
                if second.exists(BATCHES):
                    norm2_variance(second)
                if nxt.exists(BATCHES):
                    split_xt(nxt)
                add_bias(at, 3)
                add_bias(at, 4)
                if second.exists(BATCHES):
                    norm2(second)
                add_bias(at, 5)
                if before.exists(BATCHES) and nxt.exists(BATCHES):
                    residual(before, 0)
                    residual_stats(before, 0)
                if nxt.exists(BATCHES):
                    maxima(nxt)
                    negate_maxima(nxt)
                    deltas(nxt, 0)
                contexts(at, 0)
                if nxt.exists(BATCHES):
                    deltas(nxt, 1)
                context_stats(at, 0)
                contexts(at, 1)
                context_stats(at, 1)

            every_batch(dve, BATCHES, one)
            end = Batch(BATCHES // UNROLL, 0)
            before, second = end.plus(-1), end.plus(-2)
            norm1_variance(before)
            residual(second, 0)
            residual_stats(second, 0)
            norm1(before)
            residual(second, 1)
            residual_stats(second, 1)
            dve.wait_ge(stats2_ready, second.n(T, T))
            norm2_variance(second)
            norm2(second)
            affine(dve, nc.vector, before, 0)
            residual(before, 0)
            residual_stats(before, 0)
            residual(before, 1)
            residual_stats(before, 1)
            dve.wait_ge(stats2_ready, before.n(T, T))
            norm2_variance(before)
            norm2(before)

        @block.gpsimd
        def _(pool):
            nc.gpsimd.memset(ident[:], 0.0).then_inc(ident_zeroed, 1)
            nc.gpsimd.memset(minus_half[:], -0.5).then_inc(minus_half_ready, 1)
            pool.wait_ge(ident_zeroed, 1)
            nc.gpsimd.affine_select(out=ident[:], in_=ident[:], compare_op=ALU.not_equal, fill=1.0, base=0,
                                    pattern=[[-1, P]], channel_multiplier=1).then_inc(ident_ready, 1)
            pool.wait_ge(minus_half_ready, 1)
            pool.wait_ge(w_hi_ready, SELF + 1)
            nc.gpsimd.tensor_tensor(w_lo[SELF][:], w_raw[SELF][:], w_hi[SELF][:].bitcast(F32), ALU.subtract
                                    ).then_inc(w_lo_ready[SELF], 1)
            pool.wait_ge(vectors_loaded, 5 * 16)

            def split_proj(at, g):
                if g == 1:
                    pool.wait_ge(dt_lo_ready, at.n(1, 1))
                pool.wait_ge(proj_hi_ready, at.n(NSPLIT, g + 1))
                nc.gpsimd.tensor_tensor(proj_lo[:, g, :], proj[:, g, :], proj_hi[:, g, :].bitcast(F32), ALU.subtract
                                        ).then_inc(proj_lo_ready, 1)

            def triangles(at):
                blocks = dt_full[:, :, 0:T, :].bitcast(F32).rearrange("p h t l -> p h (t l)")
                for to, sign in ((dt_left, 1), (dt_right, -1)):
                    nc.gpsimd.affine_select(out=to[:].rearrange("p h t l -> p h (t l)"), in_=blocks, compare_op=ALU.is_gt, fill=0.0, base=0,
                                            pattern=[[0, 2], [0, T], [-sign, P]], channel_multiplier=sign
                                            ).then_inc(triangles_ready, 1)

            def power1(at):
                pool.wait_ge(var1_eps_ready, at.n(T, T))
                nc.gpsimd.tensor_tensor(pow1[:], var1_eps[:], minus_half[:], ALU.pow).then_inc(pow1_ready, 1)

            def power2(at):
                pool.wait_ge(var2_eps_ready, at.n(1, 1))
                nc.gpsimd.tensor_tensor(scale2[:], var2_eps[:], minus_half[:], ALU.pow).then_inc(scale2_ready, 1)

            def one(at):
                before, second = at.plus(-1), at.plus(-2)
                if before.exists(BATCHES):
                    power1(before)
                split_proj(at, 0)
                split_proj(at, 1)
                triangles(at)
                if not at.plus(1).exists(BATCHES):
                    split_proj(at, 2)
                    split_proj(at, 3)
                if second.exists(BATCHES):
                    power2(second)
                if before.exists(BATCHES):
                    affine(pool, nc.gpsimd, before, 0)
                if at.plus(1).exists(BATCHES):
                    split_proj(at, 2)
                    split_proj(at, 3)
                if before.exists(BATCHES):
                    affine(pool, nc.gpsimd, before, 1)

            every_batch(pool, BATCHES, one)
            end = Batch(BATCHES // UNROLL, 0)
            power1(end.plus(-1))
            power2(end.plus(-2))
            affine(pool, nc.gpsimd, end.plus(-1), 1)
            power2(end.plus(-1))


_INS = ["x", "x_t", "adj", "L0_gnn_W_left", "L0_gnn_b_left", "L0_gnn_W_self", "L0_gnn_b_self", "L0_gnn_W_right",
        "L0_gnn_b_right", "L0_gnn_gamma", "L0_gnn_beta"]


def kernel(**inputs):
    import numpy as _np
    import concourse.bacc as _bacc
    from concourse import mybir as _mybir
    from concourse.bass_utils import run_bass_kernel_spmd as _run

    nc = _bacc.Bacc("TRN2", target_bir_lowering=False, num_devices=1)
    arrays, args = {}, []
    for name in _INS:
        a = _np.asarray(inputs["x" if name == "x_t" else name])
        a = _np.ascontiguousarray(a.swapaxes(-1, -2) if "_W_" in name or name == "x_t" else a)
        arrays[f"in_{name}"] = a
        args.append(nc.dram_tensor(f"in_{name}", a.shape, _mybir.dt.from_np(a.dtype), kind="ExternalInput").ap())
    shape = arrays["in_x"].shape
    out = nc.dram_tensor("out_dram", shape, _mybir.dt.float32, kind="ExternalOutput").ap()
    gnn_resnorm(nc, *args, out)
    r = _run(nc, [arrays], core_ids=[0])
    return r.results[0]["out_dram"]
```
